# Optimizing a Trainium2 kernel written in Bass

```python
import numpy as np
import jax
import jax.numpy as jnp

def _softmax(x, axis=-1):
    return jax.nn.softmax(x, axis=axis)

def _gelu(x):
    return jax.nn.gelu(x, approximate=True)

def _silu(x):
    return jax.nn.silu(x)

def _sigmoid(x):
    return jax.nn.sigmoid(x)

def _layernorm(x, axis=-1, eps=1e-05):
    m = jnp.mean(x, axis=axis, keepdims=True)
    v = jnp.var(x, axis=axis, keepdims=True)
    return (x - m) / jnp.sqrt(v + eps)

def _scatter_add(tgt, idx, src, axis=0):
    return tgt.at[idx].add(src)

def _segment_sum(src, seg, n):
    return jax.ops.segment_sum(src, seg, n)
kernel_name = 'mk_dlrm_tower_d1_rec_r8_ffe6a9'

def setup_inputs(seed: int=0):
    np.random.seed(seed)
    _w = jnp.asarray

    def _rec_inputs():
        import jax
        import jax.numpy as jnp
        _tk = jax.random.key(seed)
        dense_ctx = jax.random.normal(jax.random.fold_in(_tk, 190), (1024, 16), jnp.float32)
        ids = jnp.stack([jax.random.randint(jax.random.fold_in(_tk, 200 + f), (1024,), 0, v, jnp.int32) for f, v in enumerate([1250, 1250, 1000, 125000, 12500, 12500, 1250, 125000, 125000, 1000, 1000, 12500, 12500, 12500, 1000, 1000, 1000, 1000, 1250, 1000, 1000, 1250, 1250, 1000, 1000, 12500, 12500, 1000, 1250, 12500, 1000, 1250])], axis=1)
        tbl_0 = 0.05 * jax.random.normal(jax.random.fold_in(_tk, 500 + 0), (1250, 64), jnp.float32)
        tbl_1 = 0.05 * jax.random.normal(jax.random.fold_in(_tk, 500 + 1), (1250, 64), jnp.float32)
        tbl_2 = 0.05 * jax.random.normal(jax.random.fold_in(_tk, 500 + 2), (1000, 64), jnp.float32)
        tbl_3 = 0.05 * jax.random.normal(jax.random.fold_in(_tk, 500 + 3), (125000, 64), jnp.float32)
        tbl_4 = 0.05 * jax.random.normal(jax.random.fold_in(_tk, 500 + 4), (12500, 64), jnp.float32)
        tbl_5 = 0.05 * jax.random.normal(jax.random.fold_in(_tk, 500 + 5), (12500, 64), jnp.float32)
        tbl_6 = 0.05 * jax.random.normal(jax.random.fold_in(_tk, 500 + 6), (1250, 64), jnp.float32)
        tbl_7 = 0.05 * jax.random.normal(jax.random.fold_in(_tk, 500 + 7), (125000, 64), jnp.float32)
        tbl_8 = 0.05 * jax.random.normal(jax.random.fold_in(_tk, 500 + 8), (125000, 64), jnp.float32)
        tbl_9 = 0.05 * jax.random.normal(jax.random.fold_in(_tk, 500 + 9), (1000, 64), jnp.float32)
        tbl_10 = 0.05 * jax.random.normal(jax.random.fold_in(_tk, 500 + 10), (1000, 64), jnp.float32)
        tbl_11 = 0.05 * jax.random.normal(jax.random.fold_in(_tk, 500 + 11), (12500, 64), jnp.float32)
        tbl_12 = 0.05 * jax.random.normal(jax.random.fold_in(_tk, 500 + 12), (12500, 64), jnp.float32)
        tbl_13 = 0.05 * jax.random.normal(jax.random.fold_in(_tk, 500 + 13), (12500, 64), jnp.float32)
        tbl_14 = 0.05 * jax.random.normal(jax.random.fold_in(_tk, 500 + 14), (1000, 64), jnp.float32)
        tbl_15 = 0.05 * jax.random.normal(jax.random.fold_in(_tk, 500 + 15), (1000, 64), jnp.float32)
        tbl_16 = 0.05 * jax.random.normal(jax.random.fold_in(_tk, 500 + 16), (1000, 64), jnp.float32)
        tbl_17 = 0.05 * jax.random.normal(jax.random.fold_in(_tk, 500 + 17), (1000, 64), jnp.float32)
        tbl_18 = 0.05 * jax.random.normal(jax.random.fold_in(_tk, 500 + 18), (1250, 64), jnp.float32)
        tbl_19 = 0.05 * jax.random.normal(jax.random.fold_in(_tk, 500 + 19), (1000, 64), jnp.float32)
        tbl_20 = 0.05 * jax.random.normal(jax.random.fold_in(_tk, 500 + 20), (1000, 64), jnp.float32)
        tbl_21 = 0.05 * jax.random.normal(jax.random.fold_in(_tk, 500 + 21), (1250, 64), jnp.float32)
        tbl_22 = 0.05 * jax.random.normal(jax.random.fold_in(_tk, 500 + 22), (1250, 64), jnp.float32)
        tbl_23 = 0.05 * jax.random.normal(jax.random.fold_in(_tk, 500 + 23), (1000, 64), jnp.float32)
        tbl_24 = 0.05 * jax.random.normal(jax.random.fold_in(_tk, 500 + 24), (1000, 64), jnp.float32)
        tbl_25 = 0.05 * jax.random.normal(jax.random.fold_in(_tk, 500 + 25), (12500, 64), jnp.float32)
        tbl_26 = 0.05 * jax.random.normal(jax.random.fold_in(_tk, 500 + 26), (12500, 64), jnp.float32)
        tbl_27 = 0.05 * jax.random.normal(jax.random.fold_in(_tk, 500 + 27), (1000, 64), jnp.float32)
        tbl_28 = 0.05 * jax.random.normal(jax.random.fold_in(_tk, 500 + 28), (1250, 64), jnp.float32)
        tbl_29 = 0.05 * jax.random.normal(jax.random.fold_in(_tk, 500 + 29), (12500, 64), jnp.float32)
        tbl_30 = 0.05 * jax.random.normal(jax.random.fold_in(_tk, 500 + 30), (1000, 64), jnp.float32)
        tbl_31 = 0.05 * jax.random.normal(jax.random.fold_in(_tk, 500 + 31), (1250, 64), jnp.float32)
        _rk = jax.random.fold_in(_tk, 7)
        W_top1 = 0.0441942 * jax.random.normal(jax.random.fold_in(_tk, 801), (512, 512), jnp.float32)
        W_top2 = 0.0441942 * jax.random.normal(jax.random.fold_in(_tk, 802), (512, 256), jnp.float32)
        W_top3 = 0.0625 * jax.random.normal(jax.random.fold_in(_tk, 803), (256, 1), jnp.float32)
        b_top1 = jnp.zeros((512,), jnp.float32)
        b_top2 = jnp.zeros((256,), jnp.float32)
        return (dense_ctx, ids, tbl_0, tbl_1, tbl_2, tbl_3, tbl_4, tbl_5, tbl_6, tbl_7, tbl_8, tbl_9, tbl_10, tbl_11, tbl_12, tbl_13, tbl_14, tbl_15, tbl_16, tbl_17, tbl_18, tbl_19, tbl_20, tbl_21, tbl_22, tbl_23, tbl_24, tbl_25, tbl_26, tbl_27, tbl_28, tbl_29, tbl_30, tbl_31, W_top1, b_top1, W_top2, b_top2, W_top3)
    dense_ctx, ids, tbl_0, tbl_1, tbl_2, tbl_3, tbl_4, tbl_5, tbl_6, tbl_7, tbl_8, tbl_9, tbl_10, tbl_11, tbl_12, tbl_13, tbl_14, tbl_15, tbl_16, tbl_17, tbl_18, tbl_19, tbl_20, tbl_21, tbl_22, tbl_23, tbl_24, tbl_25, tbl_26, tbl_27, tbl_28, tbl_29, tbl_30, tbl_31, W_top1, b_top1, W_top2, b_top2, W_top3 = _rec_inputs()

    def _L0_rec_setup():
        import jax, jax.numpy as jnp
        import numpy as np
        BATCH = 256
        NUM_FIELDS = 32
        EMBED = 64
        NPAIRS = NUM_FIELDS * (NUM_FIELDS - 1) // 2
        ROW, COL = np.triu_indices(NUM_FIELDS, k=1)
        ROW = jnp.asarray(ROW)
        COL = jnp.asarray(COL)
        key = jax.random.key(seed)
        k1, k2 = jax.random.split(key)
        emb_inputs = jax.random.normal(k1, (BATCH, NUM_FIELDS, EMBED), dtype=jnp.float32)
        fan_in = NPAIRS * EMBED
        fan_out = EMBED * EMBED
        std = float(np.sqrt(2.0 / (fan_in + fan_out)))
        kernel = jax.random.normal(k2, (EMBED, NPAIRS, EMBED), dtype=jnp.float32) * std
        return {'emb_inputs': emb_inputs, 'kernel': kernel}
    _L0_rec_all = _L0_rec_setup()
    _L0_rec_in = {k: v for k, v in _L0_rec_all.items() if k in ('kernel',)}
    del _L0_rec_all
    return {'dense_ctx': dense_ctx, 'ids': ids, 'tbl_0': tbl_0, 'tbl_1': tbl_1, 'tbl_2': tbl_2, 'tbl_3': tbl_3, 'tbl_4': tbl_4, 'tbl_5': tbl_5, 'tbl_6': tbl_6, 'tbl_7': tbl_7, 'tbl_8': tbl_8, 'tbl_9': tbl_9, 'tbl_10': tbl_10, 'tbl_11': tbl_11, 'tbl_12': tbl_12, 'tbl_13': tbl_13, 'tbl_14': tbl_14, 'tbl_15': tbl_15, 'tbl_16': tbl_16, 'tbl_17': tbl_17, 'tbl_18': tbl_18, 'tbl_19': tbl_19, 'tbl_20': tbl_20, 'tbl_21': tbl_21, 'tbl_22': tbl_22, 'tbl_23': tbl_23, 'tbl_24': tbl_24, 'tbl_25': tbl_25, 'tbl_26': tbl_26, 'tbl_27': tbl_27, 'tbl_28': tbl_28, 'tbl_29': tbl_29, 'tbl_30': tbl_30, 'tbl_31': tbl_31, 'W_top1': W_top1, 'b_top1': b_top1, 'W_top2': W_top2, 'b_top2': b_top2, 'W_top3': W_top3, 'L0_rec_kernel': _L0_rec_in['kernel']}

def reference(dense_ctx, ids, tbl_0, tbl_1, tbl_2, tbl_3, tbl_4, tbl_5, tbl_6, tbl_7, tbl_8, tbl_9, tbl_10, tbl_11, tbl_12, tbl_13, tbl_14, tbl_15, tbl_16, tbl_17, tbl_18, tbl_19, tbl_20, tbl_21, tbl_22, tbl_23, tbl_24, tbl_25, tbl_26, tbl_27, tbl_28, tbl_29, tbl_30, tbl_31, W_top1, b_top1, W_top2, b_top2, W_top3, L0_rec_kernel):
    import jax
    import jax.numpy as jnp

    def _L0_rec_ref(emb_inputs, kernel):
        import jax, jax.numpy as jnp
        import numpy as np
        BATCH = 256
        NUM_FIELDS = 32
        EMBED = 64
        NPAIRS = NUM_FIELDS * (NUM_FIELDS - 1) // 2
        ROW, COL = np.triu_indices(NUM_FIELDS, k=1)
        ROW = jnp.asarray(ROW)
        COL = jnp.asarray(COL)
        p = emb_inputs[:, ROW]
        q = emb_inputs[:, COL]
        kp = jnp.einsum('bpj,ipj->bpi', p, kernel)
        outputs = jnp.sum(kp * q, axis=-1)
        return outputs[:, None, :]
    e = jnp.stack([tbl_0[ids[:, 0]], tbl_1[ids[:, 1]], tbl_2[ids[:, 2]], tbl_3[ids[:, 3]], tbl_4[ids[:, 4]], tbl_5[ids[:, 5]], tbl_6[ids[:, 6]], tbl_7[ids[:, 7]], tbl_8[ids[:, 8]], tbl_9[ids[:, 9]], tbl_10[ids[:, 10]], tbl_11[ids[:, 11]], tbl_12[ids[:, 12]], tbl_13[ids[:, 13]], tbl_14[ids[:, 14]], tbl_15[ids[:, 15]], tbl_16[ids[:, 16]], tbl_17[ids[:, 17]], tbl_18[ids[:, 18]], tbl_19[ids[:, 19]], tbl_20[ids[:, 20]], tbl_21[ids[:, 21]], tbl_22[ids[:, 22]], tbl_23[ids[:, 23]], tbl_24[ids[:, 24]], tbl_25[ids[:, 25]], tbl_26[ids[:, 26]], tbl_27[ids[:, 27]], tbl_28[ids[:, 28]], tbl_29[ids[:, 29]], tbl_30[ids[:, 30]], tbl_31[ids[:, 31]]], axis=1)
    z = _L0_rec_ref(e, L0_rec_kernel)
    z = z.reshape(z.shape[0], -1)
    h = jnp.concatenate([z, dense_ctx], axis=1)
    h = jnp.maximum(h @ W_top1 + b_top1, 0.0)
    h = jnp.maximum(h @ W_top2 + b_top2, 0.0)
    y = h @ W_top3
    return y

_drawn_inputs = setup_inputs


def setup_inputs(seed=0):
    import zlib

    import numpy as np

    out = dict(_drawn_inputs(seed))
    spreads = {'b_top1': (0.0, 0.1), 'b_top2': (0.0, 0.1)}
    factors = {'tbl_0': 8.0,
     'tbl_1': 8.0,
     'tbl_2': 8.0,
     'tbl_3': 8.0,
     'tbl_4': 8.0,
     'tbl_5': 8.0,
     'tbl_6': 8.0,
     'tbl_7': 8.0,
     'tbl_8': 8.0,
     'tbl_9': 8.0,
     'tbl_10': 8.0,
     'tbl_11': 8.0,
     'tbl_12': 8.0,
     'tbl_13': 8.0,
     'tbl_14': 8.0,
     'tbl_15': 8.0,
     'tbl_16': 8.0,
     'tbl_17': 8.0,
     'tbl_18': 8.0,
     'tbl_19': 8.0,
     'tbl_20': 8.0,
     'tbl_21': 8.0,
     'tbl_22': 8.0,
     'tbl_23': 8.0,
     'tbl_24': 8.0,
     'tbl_25': 8.0,
     'tbl_26': 8.0,
     'tbl_27': 8.0,
     'tbl_28': 8.0,
     'tbl_29': 8.0,
     'tbl_30': 8.0,
     'tbl_31': 8.0,
     'L0_rec_kernel': 8.0}
    for name, (base, spread) in spreads.items():
        noise = np.random.default_rng([zlib.crc32(name.encode()), seed]).standard_normal(out[name].shape)
        drawn = base * np.exp(spread * noise) if base else spread * noise
        out[name] = jnp.asarray(drawn.astype(out[name].dtype))
    for name, factor in factors.items():
        out[name] = (out[name] * factor).astype(out[name].dtype)
    return out
```

```python
import numpy as np
import concourse.bass as bass
import concourse.mybir as mybir

F32 = mybir.dt.float32
F32R = mybir.dt.float32r
I32 = mybir.dt.int32
ALU = mybir.AluOpType
ACT = mybir.ActivationFunctionType

BATCH, FIELDS, EMBED, DENSE = 1024, 32, 64, 16
HID1, HID2 = 512, 256
P = 128
HALVES = 2
ROWS = BATCH // HALVES
RB = ROWS // P
GROUPS = FIELDS // 2
TILES = GROUPS * GROUPS
CHUNK = 16
CHUNKS = TILES // CHUNK
SLOT = 2
SLOTS = TILES // SLOT
BATCH_SLOTS = 2
BATCHES = SLOTS // BATCH_SLOTS
TILES_PER_BATCH = SLOT * BATCH_SLOTS
FEATURES = 2 * TILES
FC = FEATURES // P
BATCHES_PER_FC = BATCHES // FC
N1, N2 = HID1 // P, HID2 // P
MLP_UNITS = N1 + N2 + 1
KP_RING = 3
assert (SLOTS + MLP_UNITS) % KP_RING == 0
P_RING = 4
RAW_RING = 4
ROUNDS = 3
K_RING = 2

TILE = [(o, k) for k in range(GROUPS) for o in range(2 * k + 1)]
assert len(TILE) == TILES


def first_batch(k):
    return k * k // TILES_PER_BATCH


def transposes_at():
    at = [[] for _ in range(BATCHES)]
    for k in range(GROUPS):
        for r in range(ROUNDS):
            lead = ROUNDS - r if k >= 6 else 0
            at[first_batch(k) - lead].append((k, r))
    assert [kr for now in at for kr in now] == [(k, r) for k in range(GROUPS) for r in range(ROUNDS)]
    return at


def feature_place(t, h):
    in_chunk = t % (TILES // FC)
    return t // (TILES // FC), 32 * (t % 4) + 2 * (in_chunk // 4) + h


def pairwise_tower(nc, dense_t, ids, tables, kd, w1, b1, w2, b2, w3, sel_dense, out):
    from contextlib import ExitStack
    ctx = ExitStack()
    with ctx:
        def sb(name, shape, dt=F32):
            return ctx.enter_context(nc.sbuf_tensor(name, shape, dt))

        def sem(name):
            return ctx.enter_context(nc.semaphore(name))

        ids_sb = sb("ids_sb", [P, RB * FIELDS], I32)
        raw = sb("raw", [P, RAW_RING, RB, 2, EMBED])
        parts = sb("parts", [P, 2, RB, 2, 2, EMBED])
        own = sb("own", [P, FIELDS, ROWS], F32R)
        pair = sb("pair", [P, GROUPS, ROWS])
        ksplit = sb("ksplit", [P, K_RING, 2, CHUNK // 2, P])
        kst = sb("kst", [P, K_RING, 2, 2, CHUNK // 2, P], F32R)
        prod = sb("prod", [P, P_RING, SLOT, ROWS])
        z_sb = sb("z_sb", [P, FC, ROWS])
        w1_sb = sb("w1_sb", [P, FC, HID1])
        w2_sb = sb("w2_sb", [P, N1, HID2])
        w3_sb = sb("w3_sb", [P, N2])
        b1_sb = sb("b1_sb", [P, N1])
        b2_sb = sb("b2_sb", [P, N2])
        dense_sb = sb("dense_sb", [DENSE, BATCH])
        seld_sb = sb("seld_sb", [DENSE, FC, P])
        ident = sb("ident", [P, P])
        ones_sel = sb("ones_sel", [P, 64])
        y_sb = sb("y_sb", [1, BATCH])
        h1_sb = prod[:, 0:2, :, :].rearrange("p a b n -> p (a b) n")
        h2_sb = prod[:, 2, :, :]

        kp = [ctx.enter_context(nc.psum_tensor(f"kp{i}", [P, SLOT, ROWS], F32)) for i in range(KP_RING)]
        z_ps = ctx.enter_context(nc.psum_tensor("z_ps", [P, ROWS], F32))
        tr_ps = ctx.enter_context(nc.psum_tensor("tr_ps", [P, ROWS], F32))

        weights_in = sem("weights_in")
        dense_in = sem("dense_in")
        ids_in = sem("ids_in")
        raw_in = [sem(f"raw_in{i}") for i in range(RAW_RING)]
        k_in = [sem(f"k_in{i}") for i in range(K_RING)]
        kst_in = [sem(f"kst_in{i}") for i in range(K_RING)]
        consts_ready = sem("consts_ready")
        khi_done = sem("khi_done")
        klo_done = sem("klo_done")
        ghi_done = sem("ghi_done")
        glo_done = sem("glo_done")
        transposed = sem("transposed")
        evacuated = sem("evacuated")
        kp_done = sem("kp_done")
        prod_done = sem("prod_done")
        reduced = sem("reduced")
        z_out = sem("z_out")
        mlp_done = sem("mlp_done")
        mlp_out = sem("mlp_out")
        y_stored = sem("y_stored")
        passed = sem("passed")

        TR0 = ROUNDS * RAW_RING
        KP0 = K_RING * CHUNK // SLOT
        RED0 = P_RING // BATCH_SLOTS
        MO0 = MLP_UNITS
        EV0 = Z0 = 1

        def wait_alone(eng, signal, n):
            eng.wait_ge(signal, n)
            eng.sem_inc(passed, 1)

        at_batch = transposes_at()
        KD2 = kd.rearrange("c p (m n) -> c p m n", n=P)

        block = ctx.enter_context(nc.Block())

        @block.sync
        def _(sp):
            def load_k(c):
                sp.dma_start(ksplit[:, c % K_RING, 1, :, :], KD2[c]).then_inc(k_in[c % K_RING], 16)

            for c in range(K_RING):
                load_k(c)
            sp.dma_start(seld_sb[:, :, :], sel_dense).then_inc(dense_in, 16)
            sp.dma_start(dense_sb[:, :], dense_t).then_inc(dense_in, 16)
            sp.dma_start(w1_sb[:, :, :], w1).then_inc(weights_in, 16)
            sp.dma_start(w2_sb[:, :, :], w2).then_inc(weights_in, 16)
            sp.dma_start(w3_sb[:, :], w3).then_inc(weights_in, 16)
            sp.dma_start(b1_sb[:, :], b1).then_inc(weights_in, 16)
            sp.dma_start(b2_sb[:, :], b2).then_inc(weights_in, 16)
            with sp.Fori(0, HALVES) as h:
                for c in range(CHUNKS):
                    i = c % K_RING
                    wait_alone(sp, klo_done, h * CHUNKS + c + 1)
                    sp.wait_ge(kp_done, h * SLOTS + KP0 + (c - K_RING + 1) * CHUNK // SLOT)
                    for q in range(2):
                        for half in range(2):
                            sp.dma_start(kst[64 * half:64 * half + 64, i, :, q, :, :].bitcast(F32),
                                         ksplit[64 * q:64 * q + 64, i, :, :, :]).then_inc(kst_in[i], 16)
                    wait_alone(sp, kst_in[i], (h * (CHUNKS // K_RING) + c // K_RING + 1) * 64)
                    if c + K_RING < CHUNKS:
                        load_k(c + K_RING)
                    else:
                        with sp.If(h < HALVES - 1):
                            load_k(c + K_RING - CHUNKS)

        @block.gpsimd
        def _(pool):
            nc.gpsimd.memset(ident[:, :], 0.0).then_inc(consts_ready, 1)
            nc.gpsimd.memset(ones_sel[:, :], 0.0).then_inc(consts_ready, 1)
            pool.wait_ge(consts_ready, 2)
            nc.gpsimd.affine_select(out=ident[:, :], in_=ident[:, :], compare_op=ALU.not_equal, fill=1.0,
                                    base=0, pattern=[[-1, P]], channel_multiplier=1).then_inc(consts_ready, 1)
            pool.wait_ge(consts_ready, 3)
            nc.gpsimd.memset(ones_sel[0:64, 30:31], 1.0).then_inc(consts_ready, 1)
            pool.wait_ge(consts_ready, 4)
            nc.gpsimd.memset(ones_sel[64:128, 31:32], 1.0).then_inc(consts_ready, 1)
            pool.wait_ge(consts_ready, 5)
            with pool.Fori(0, HALVES) as h:
                pool.dma_start(ids_sb[:, :], ids[h]).then_inc(ids_in, 16)
                wait_alone(pool, ids_in, h * 16 + 16)
                for k in range(GROUPS):
                    wait_alone(pool, transposed, h * GROUPS * ROUNDS + TR0 + (k - RAW_RING + 1) * ROUNDS)
                    for n in range(2):
                        f = 2 * k + n
                        for b in range(RB):
                            col = b * FIELDS + f
                            nc.gpsimd.indirect_dma_start(
                                raw[:, k % RAW_RING, b, n, :], None, tables[f],
                                bass.IndirectOffsetOnAxis(ap=ids_sb[:, col:col + 1], axis=0),
                            ).then_inc(raw_in[k % RAW_RING], 16)
                for i in range(RAW_RING):
                    wait_alone(pool, raw_in[i], (h + 1) * (GROUPS // RAW_RING) * 2 * RB * 16)

        def wait_raw(eng, h, k):
            eng.wait_ge(raw_in[k % RAW_RING],
                        h * (GROUPS // RAW_RING) * 2 * RB * 16 + (k // RAW_RING + 1) * 2 * RB * 16)

        @block.scalar
        def _(act):
            act.sem_inc(mlp_out, MO0)
            act.sem_inc(evacuated, EV0)
            act.sem_inc(z_out, Z0)
            act.wait_ge(weights_in, 5 * 16)

            def k_high(n, i, m):
                act.wait_ge(k_in[i], n)
                nc.scalar.activation(ksplit[:, i, 0, :, :].bitcast(F32R), ksplit[:, i, 1, :, :],
                                     ACT.Copy).then_inc(khi_done, 1)

            def g_high(h, k):
                wait_raw(act, h, k)
                act.wait_ge(transposed, h * GROUPS * ROUNDS + TR0 + (k - 2) * ROUNDS + 2)
                nc.scalar.activation(parts[:, k % 2, :, :, 0, :].bitcast(F32R), raw[:, k % RAW_RING, :, :, :],
                                     ACT.Copy).then_inc(ghi_done, 1)

            def evacuate(h, k, r):
                act.wait_ge(transposed, h * GROUPS * ROUNDS + TR0 + k * ROUNDS + r + 1)
                dst = own[:, 2 * k + r, :] if r < 2 else pair[:, k, :]
                nc.scalar.activation(dst, tr_ps[:, :], ACT.Copy).then_inc(evacuated, 1)

            for c in range(K_RING):
                k_high(16, c, c)
            with act.Fori(0, HALVES) as h:
                for j in range(BATCHES):
                    for k, r in at_batch[j]:
                        if r == 0:
                            g_high(h, k)
                        evacuate(h, k, r)
                    if j and j % BATCHES_PER_FC == 0:
                        act.wait_ge(reduced, h * BATCHES + RED0 + j)
                        nc.scalar.activation(z_sb[:, j // BATCHES_PER_FC - 1, :], z_ps[:, :],
                                             ACT.Copy).then_inc(z_out, 1)
                    if j % (CHUNK // TILES_PER_BATCH) == 1:
                        c = j // (CHUNK // TILES_PER_BATCH) + K_RING
                        i = c % K_RING
                        n = h * (CHUNKS // K_RING) * 16 + (c // K_RING + 1) * 16
                        if c < CHUNKS:
                            k_high(n, i, c)
                        else:
                            with act.If(h < HALVES - 1):
                                k_high(n, i, c)
                act.wait_ge(reduced, h * BATCHES + RED0 + BATCHES)
                nc.scalar.activation(z_sb[:, FC - 1, :], z_ps[:, :], ACT.Copy).then_inc(z_out, 1)
                for u in range(MLP_UNITS):
                    act.wait_ge(mlp_done, h * MLP_UNITS + u + 1)
                    src = kp[(SLOTS + u) % KP_RING]
                    if u < N1:
                        nc.scalar.activation(h1_sb[:, u, :], src[:, 0, :], ACT.Relu,
                                             bias=b1_sb[:, u:u + 1]).then_inc(mlp_out, 1)
                    elif u < N1 + N2:
                        nc.scalar.activation(h2_sb[:, u - N1, :], src[:, 0, :], ACT.Relu,
                                             bias=b2_sb[:, u - N1:u - N1 + 1]).then_inc(mlp_out, 1)
                    else:
                        nc.scalar.activation(y_sb[0:1, bass.ds(h * ROWS, ROWS)], src[0:1, 0, :],
                                             ACT.Copy).then_inc(mlp_out, 1)
            act.wait_ge(mlp_out, HALVES * MLP_UNITS + MO0)
            act.dma_start(out, y_sb[0:1, :]).then_inc(y_stored, 16)
            act.wait_ge(y_stored, 16)

        @block.vector
        def _(dve):
            def k_low(n, i):
                dve.wait_ge(khi_done, n)
                nc.vector.tensor_tensor(ksplit[:, i, 1, :, :].bitcast(F32R), ksplit[:, i, 1, :, :],
                                        ksplit[:, i, 0, :, :], ALU.subtract).then_inc(klo_done, 1)

            def g_low(h, k):
                dve.wait_ge(ghi_done, h * GROUPS + k + 1)
                nc.vector.tensor_tensor(parts[:, k % 2, :, :, 1, :].bitcast(F32R), raw[:, k % RAW_RING, :, :, :],
                                        parts[:, k % 2, :, :, 0, :], ALU.subtract).then_inc(glo_done, 1)

            for c in range(K_RING):
                k_low(c + 1, c)
            with dve.Fori(0, HALVES) as h:
                for j in range(BATCHES):
                    for k, r in at_batch[j]:
                        if r == 0:
                            g_low(h, k)
                    for s in range(BATCH_SLOTS * j, BATCH_SLOTS * (j + 1)):
                        k0, k1 = TILE[SLOT * s][1], TILE[SLOT * s + 1][1]
                        if k0 == k1:
                            factor = pair[:, k0:k0 + 1, :].broadcast_to([P, SLOT, ROWS])
                        else:
                            factor = pair[:, k0:k0 + SLOT, :]
                        dve.wait_ge(kp_done, h * SLOTS + KP0 + s + 1)
                        if s % BATCH_SLOTS == 0:
                            dve.wait_ge(reduced, h * BATCHES + RED0 + j + 1 - P_RING // BATCH_SLOTS)
                        nc.vector.tensor_tensor(prod[:, s % P_RING, :, :], kp[s % KP_RING][:, :, :],
                                                factor, ALU.mult).then_inc(prod_done, 1)
                    if j % (CHUNK // TILES_PER_BATCH) == 1:
                        c = j // (CHUNK // TILES_PER_BATCH) + K_RING
                        if c < CHUNKS:
                            k_low(h * CHUNKS + c + 1, c % K_RING)
                        else:
                            with dve.If(h < HALVES - 1):
                                k_low(h * CHUNKS + c + 1, c % K_RING)

        @block.tensor
        def _(pe):
            pe.sem_inc(transposed, TR0)
            pe.sem_inc(kp_done, KP0)
            pe.sem_inc(reduced, RED0)
            pe.wait_ge(consts_ready, 5)
            pe.wait_ge(dense_in, 2 * 16)

            def transpose_round(h, k, r):
                if r == 0:
                    pe.wait_ge(glo_done, h * GROUPS + k + 1)
                pe.wait_ge(evacuated, h * GROUPS * ROUNDS + EV0 + k * ROUNDS + r)
                for b in range(RB):
                    if r < 2:
                        src = parts[:, k % 2, b, r, :, :].rearrange("p a n -> p (a n)")
                    else:
                        src = raw[:, k % RAW_RING, b, :, :].rearrange("p a n -> p (a n)")
                    last = nc.tensor.transpose(tr_ps[:, b * P:(b + 1) * P], src, ident[:, :])
                last.then_inc(transposed, 1)

            def kp_free(h, s):
                if s < KP_RING:
                    pe.wait_ge(mlp_out, h * MLP_UNITS + MO0 + s - KP_RING + 1)
                elif s - KP_RING < SLOTS:
                    pe.wait_ge(prod_done, h * SLOTS + s - KP_RING + 1)
                else:
                    pe.wait_ge(mlp_out, h * MLP_UNITS + MO0 + s - KP_RING - SLOTS + 1)

            def products(h, s):
                kp_free(h, s)
                for q in range(SLOT):
                    t = SLOT * s + q
                    o, k = TILE[t]
                    c = t // CHUNK
                    if t % CHUNK == 0:
                        pe.wait_ge(kst_in[c % K_RING], (h * (CHUNKS // K_RING) + c // K_RING + 1) * 64)
                    if o == 0:
                        pe.wait_ge(evacuated, h * GROUPS * ROUNDS + EV0 + (k + 1) * ROUNDS)
                    for part in range(2):
                        last = nc.tensor.matmul(kp[s % KP_RING][:, q, :],
                                                kst[:, c % K_RING, part, t % 2, (t % CHUNK) // 2, :],
                                                own[:, o, :], start=(part == 0), stop=(part == 1))
                last.then_inc(kp_done, 1)

            def reductions(h, j):
                if j % BATCHES_PER_FC == 0:
                    c = j // BATCHES_PER_FC
                    wait_alone(pe, z_out, h * FC + Z0 + c)
                    nc.tensor.matmul(z_ps[:, :], seld_sb[:, c, :], dense_sb[:, bass.ds(h * ROWS, ROWS)],
                                     start=True, stop=False, skip_group_check=True)
                pe.wait_ge(prod_done, h * SLOTS + BATCH_SLOTS * (j + 1))
                for t in range(TILES_PER_BATCH * j, TILES_PER_BATCH * (j + 1)):
                    g = t % 4
                    col = 2 * ((t % (TILES // FC)) // 4)
                    s = t // SLOT
                    last = nc.tensor.matmul(z_ps[32 * g:32 * g + 32, :], ones_sel[:, 30 - col:62 - col],
                                            prod[:, s % P_RING, t % SLOT, :], start=False,
                                            stop=(j % BATCHES_PER_FC == BATCHES_PER_FC - 1),
                                            skip_group_check=True)
                last.then_inc(reduced, 1)

            with pe.Fori(0, HALVES) as h:
                for j in range(BATCHES):
                    for k, r in at_batch[j]:
                        transpose_round(h, k, r)
                    for s in range(BATCH_SLOTS * j, BATCH_SLOTS * (j + 1)):
                        products(h, s)
                    if j:
                        reductions(h, j - 1)
                reductions(h, BATCHES - 1)
                pe.wait_ge(z_out, (h + 1) * FC + Z0)
                pe.wait_ge(weights_in, 5 * 16)
                for u in range(MLP_UNITS):
                    s = SLOTS + u
                    kp_free(h, s)
                    dst = kp[s % KP_RING]
                    if u < N1:
                        for c in range(FC):
                            last = nc.tensor.matmul(dst[:, 0, :], w1_sb[:, c, u * P:(u + 1) * P], z_sb[:, c, :],
                                                    start=(c == 0), stop=(c == FC - 1))
                    elif u < N1 + N2:
                        pe.wait_ge(mlp_out, h * MLP_UNITS + MO0 + N1)
                        n = u - N1
                        for c in range(N1):
                            last = nc.tensor.matmul(dst[:, 0, :], w2_sb[:, c, n * P:(n + 1) * P], h1_sb[:, c, :],
                                                    start=(c == 0), stop=(c == N1 - 1))
                    else:
                        pe.wait_ge(mlp_out, h * MLP_UNITS + MO0 + N1 + N2)
                        for c in range(N2):
                            last = nc.tensor.matmul(dst[0:1, 0, :], w3_sb[:, c:c + 1], h2_sb[:, c, :],
                                                    start=(c == 0), stop=(c == N2 - 1))
                    last.then_inc(mlp_done, 1)


def kernel(**inputs):
    import numpy as _np
    import concourse.bacc as _bacc
    from concourse import mybir as _mybir
    from concourse.bass_utils import run_bass_kernel_spmd as _run

    pair_no = {}
    for r in range(FIELDS):
        for c in range(r + 1, FIELDS):
            pair_no[(r, c)] = len(pair_no)
    pairs = len(pair_no)
    k_order = _np.zeros((TILES, 2), _np.int64)
    w1_rows = _np.zeros((FC, P), _np.int64)
    sel = _np.zeros((DENSE, FC, P), _np.float32)
    for t, (o, k) in enumerate(TILE):
        for h in range(2):
            c, row = feature_place(t, h)
            if (o, 2 * k + h) in pair_no:
                k_order[t, h] = pair_no[(o, 2 * k + h)]
                w1_rows[c, row] = pair_no[(o, 2 * k + h)]
            else:
                k_order[t, h] = pairs
                w1_rows[c, row] = pairs + k
                sel[k, c, row] = 1.0
    kt = _np.asarray(inputs["L0_rec_kernel"]).transpose(2, 1, 0)
    kt = _np.concatenate([kt, _np.zeros((EMBED, 1, EMBED), kt.dtype)], axis=1)
    kt = kt[:, k_order.reshape(-1), :].reshape(EMBED, CHUNKS, CHUNK // 2, 2, 2, EMBED)
    kd = kt.transpose(1, 3, 0, 2, 4, 5).reshape(CHUNKS, P, CHUNK // 2 * P)
    w1 = _np.asarray(inputs["W_top1"])[w1_rows.reshape(-1)].reshape(FC, P, HID1).transpose(1, 0, 2)
    w2 = _np.asarray(inputs["W_top2"]).reshape(N1, P, HID2).transpose(1, 0, 2)
    w3 = _np.asarray(inputs["W_top3"]).reshape(N2, P).transpose(1, 0)
    b1 = _np.asarray(inputs["b_top1"]).reshape(N1, P).transpose(1, 0)
    b2 = _np.asarray(inputs["b_top2"]).reshape(N2, P).transpose(1, 0)
    ids = _np.asarray(inputs["ids"]).reshape(HALVES, RB, P, FIELDS).transpose(0, 2, 1, 3)
    arrays = {
        "dense_t": _np.asarray(inputs["dense_ctx"]).transpose(1, 0),
        "ids": ids.reshape(HALVES, P, RB * FIELDS),
    }
    for f in range(FIELDS):
        arrays[f"tbl_{f}"] = _np.asarray(inputs[f"tbl_{f}"])
    arrays.update(kd=kd, w1=w1, b1=b1, w2=w2, b2=b2, w3=w3, sel_dense=sel)

    nc = _bacc.Bacc("TRN2", target_bir_lowering=False, num_devices=1)
    feed, ap = {}, {}
    for name, a in arrays.items():
        a = _np.ascontiguousarray(a)
        feed[f"in_{name}"] = a
        ap[name] = nc.dram_tensor(f"in_{name}", a.shape, _mybir.dt.from_np(a.dtype), kind="ExternalInput").ap()
    out = nc.dram_tensor("out_y", (1, BATCH), _mybir.dt.float32, kind="ExternalOutput").ap()
    pairwise_tower(nc, ap["dense_t"], ap["ids"], [ap[f"tbl_{f}"] for f in range(FIELDS)], ap["kd"], ap["w1"],
                   ap["b1"], ap["w2"], ap["b2"], ap["w3"], ap["sel_dense"], out)
    r = _run(nc, [feed], core_ids=[0])
    return r.results[0]["out_y"].reshape(BATCH, 1)
```

```python
import numpy as np
import concourse.bass as bass
import concourse.mybir as mybir

F32 = mybir.dt.float32
F32R = mybir.dt.float32r
I32 = mybir.dt.int32
ALU = mybir.AluOpType
ACT = mybir.ActivationFunctionType

BATCH, FIELDS, EMBED, DENSE = 1024, 32, 64, 16
HID1, HID2 = 512, 256
P = 128
HALVES = 2
ROWS = BATCH // HALVES
RB = ROWS // P
GROUPS = FIELDS // 2
TILES = GROUPS * GROUPS
CHUNK = 16
CHUNKS = TILES // CHUNK
SLOT = 2
SLOTS = TILES // SLOT
BATCH_SLOTS = 2
BATCHES = SLOTS // BATCH_SLOTS
TILES_PER_BATCH = SLOT * BATCH_SLOTS
FEATURES = 2 * TILES
FC = FEATURES // P
BATCHES_PER_FC = BATCHES // FC
N1, N2 = HID1 // P, HID2 // P
MLP_UNITS = N1 + N2 + 1
KP_RING = 3
assert (SLOTS + MLP_UNITS) % KP_RING == 0
P_RING = 4
RAW_RING = 4
SPLIT_RING = 2
EARLY = 2
K_RING = 2
LEAD_EARLY, LEAD_LATE = 1, 3

TILE = [(o, k) for k in range(GROUPS) for o in range(2 * k + 1)]
assert len(TILE) == TILES


def first_batch(k):
    return k * k // TILES_PER_BATCH


def groups_at():
    at = [[] for _ in range(BATCHES)]
    for k in range(EARLY, GROUPS):
        at[first_batch(k) - (LEAD_LATE if k >= 6 else LEAD_EARLY)].append(k)
    assert [k for now in at for k in now] == list(range(EARLY, GROUPS))
    return at


def feature_place(t, h):
    in_chunk = t % (TILES // FC)
    return t // (TILES // FC), 32 * (t % 4) + 2 * (in_chunk // 4) + h


def pairwise_tower(nc, dense, ids, tables, kd, w1, b1, w2, b2, w3, out):
    from contextlib import ExitStack
    ctx = ExitStack()
    with ctx:
        def sb(name, shape, dt=F32):
            return ctx.enter_context(nc.sbuf_tensor(name, shape, dt))

        def sem(name):
            return ctx.enter_context(nc.semaphore(name))

        ids_sb = sb("ids_sb", [P, RB * FIELDS], I32)
        raw = sb("raw", [P, RAW_RING, RB, 2, EMBED])
        split = sb("split", [P, SPLIT_RING, 2, ROWS])
        own = sb("own", [P, FIELDS, ROWS], F32R)
        pair = sb("pair", [P, GROUPS, ROWS])
        ksplit = sb("ksplit", [P, K_RING, 2, CHUNK // 2, P])
        kst = sb("kst", [P, K_RING, 2, 2, CHUNK // 2, P], F32R)
        prod = sb("prod", [P, P_RING, SLOT, ROWS])
        z_sb = sb("z_sb", [P, FC, ROWS])
        w1_sb = sb("w1_sb", [P, FC, HID1])
        w2_sb = sb("w2_sb", [P, N1, HID2])
        w3_sb = sb("w3_sb", [P, N2])
        b1_sb = sb("b1_sb", [P, N1])
        b2_sb = sb("b2_sb", [P, N2])
        ident = sb("ident", [P, P])
        ones_sel = sb("ones_sel", [P, 64])
        y_sb = sb("y_sb", [1, BATCH])
        h1_sb = prod[:, 0:2, :, :].rearrange("p a b n -> p (a b) n")
        h2_sb = prod[:, 2, :, :]

        kp = [ctx.enter_context(nc.psum_tensor(f"kp{i}", [P, SLOT, ROWS], F32)) for i in range(KP_RING)]
        z_ps = ctx.enter_context(nc.psum_tensor("z_ps", [P, ROWS], F32))
        tr_ps = ctx.enter_context(nc.psum_tensor("tr_ps", [P, ROWS], F32))

        weights_in = sem("weights_in")
        dense_in = sem("dense_in")
        ids_in = sem("ids_in")
        raw_in = [sem(f"raw_in{i}") for i in range(RAW_RING)]
        k_in = [sem(f"k_in{i}") for i in range(K_RING)]
        kst_in = [sem(f"kst_in{i}") for i in range(K_RING)]
        consts_ready = sem("consts_ready")
        khi_done = sem("khi_done")
        klo_done = sem("klo_done")
        own_in = [sem(f"own_in{i}") for i in range(SPLIT_RING)]
        glo_done = sem("glo_done")
        transposed = sem("transposed")
        evacuated = sem("evacuated")
        kp_done = sem("kp_done")
        prod_done = sem("prod_done")
        reduced = sem("reduced")
        z_out = sem("z_out")
        mlp_done = sem("mlp_done")
        mlp_out = sem("mlp_out")
        y_stored = sem("y_stored")
        passed = sem("passed")

        TR0 = RAW_RING
        KP0 = CHUNK // SLOT
        RED0 = P_RING // BATCH_SLOTS
        MO0 = MLP_UNITS
        EV0 = Z0 = 1
        CB = CHUNK // TILES_PER_BATCH

        def wait_alone(eng, signal, n):
            eng.wait_ge(signal, n)
            eng.sem_inc(passed, 1)

        at_batch = groups_at()
        KD2 = kd.rearrange("c p (m n) -> c p m n", n=P)

        def in_next_half(eng, h, other_half, step):
            if other_half:
                with eng.If(h < HALVES - 1):
                    step()
            else:
                step()

        block = ctx.enter_context(nc.Block())

        @block.sync
        def _(sp):
            def load_k(c):
                sp.dma_start(ksplit[:, c % K_RING, 1, :, :], KD2[c]).then_inc(k_in[c % K_RING], 16)

            def load_dense(h):
                sp.dma_start(z_sb[:, :, :], dense[h]).then_inc(dense_in, 16)

            def spread_k(h, c):
                i = c % K_RING
                wait_alone(sp, klo_done, h * CHUNKS + c + 1)
                for q in range(2):
                    for half in range(2):
                        sp.dma_start(kst[64 * half:64 * half + 64, i, :, q, :, :].bitcast(F32),
                                     ksplit[64 * q:64 * q + 64, i, :, :, :]).then_inc(kst_in[i], 16)

            def spread_own(h, k):
                wait_alone(sp, glo_done, h * GROUPS + k + 1)
                for n in range(2):
                    for part in range(2):
                        sp.dma_start(own[64 * part:64 * part + 64, 2 * k + n, :].bitcast(F32),
                                     split[64 * n:64 * n + 64, k % SPLIT_RING, part, :],
                                     ).then_inc(own_in[k % SPLIT_RING], 16)

            def spread_read(h, c):
                wait_alone(sp, kst_in[c % K_RING], (h * (CHUNKS // K_RING) + c // K_RING + 1) * 64)

            load_k(0)
            load_k(1)
            spread_k(0, 0)
            load_dense(0)
            for k in range(EARLY):
                spread_own(0, k)
            spread_read(0, 0)
            load_k(2)
            sp.dma_start(w1_sb[:, :, :], w1).then_inc(weights_in, 16)
            sp.dma_start(w2_sb[:, :, :], w2).then_inc(weights_in, 16)
            sp.dma_start(w3_sb[:, :], w3).then_inc(weights_in, 16)
            sp.dma_start(b1_sb[:, :], b1).then_inc(weights_in, 16)
            sp.dma_start(b2_sb[:, :], b2).then_inc(weights_in, 16)
            with sp.Fori(0, HALVES) as h:
                for j in range(BATCHES):
                    if j % CB == 0:
                        dh, c = divmod(j // CB + 1, CHUNKS)
                        wait_alone(sp, kp_done, h * SLOTS + KP0 + j // CB * CHUNK // SLOT)
                        in_next_half(sp, h, dh, lambda: spread_k(h + dh, c))
                    for k in at_batch[j]:
                        spread_own(h, k)
                    if j % CB == 2:
                        dh, c = divmod(j // CB + 1, CHUNKS)
                        dn, n = divmod(j // CB + 1 + K_RING, CHUNKS)

                        def next_load():
                            spread_read(h + dh, c)
                            load_k(n)
                        in_next_half(sp, h, dn, next_load)
                with sp.If(h < HALVES - 1):
                    for k in range(EARLY):
                        spread_own(h + 1, k)
                    wait_alone(sp, mlp_done, h * MLP_UNITS + N1)
                    load_dense(HALVES - 1)

        @block.gpsimd
        def _(pool):
            nc.gpsimd.memset(ident[:, :], 0.0).then_inc(consts_ready, 1)
            nc.gpsimd.memset(ones_sel[:, :], 0.0).then_inc(consts_ready, 1)
            pool.wait_ge(consts_ready, 2)
            nc.gpsimd.affine_select(out=ident[:, :], in_=ident[:, :], compare_op=ALU.not_equal, fill=1.0,
                                    base=0, pattern=[[-1, P]], channel_multiplier=1).then_inc(consts_ready, 1)
            pool.wait_ge(consts_ready, 3)
            nc.gpsimd.memset(ones_sel[0:64, 30:31], 1.0).then_inc(consts_ready, 1)
            pool.wait_ge(consts_ready, 4)
            nc.gpsimd.memset(ones_sel[64:128, 31:32], 1.0).then_inc(consts_ready, 1)
            pool.wait_ge(consts_ready, 5)
            with pool.Fori(0, HALVES) as h:
                pool.dma_start(ids_sb[:, :], ids[h]).then_inc(ids_in, 16)
                wait_alone(pool, ids_in, h * 16 + 16)
                for k in range(GROUPS):
                    wait_alone(pool, transposed, h * GROUPS + TR0 + k - RAW_RING + 1)
                    for n in range(2):
                        f = 2 * k + n
                        for b in range(RB):
                            col = b * FIELDS + f
                            nc.gpsimd.indirect_dma_start(
                                raw[:, k % RAW_RING, b, n, :], None, tables[f],
                                bass.IndirectOffsetOnAxis(ap=ids_sb[:, col:col + 1], axis=0),
                            ).then_inc(raw_in[k % RAW_RING], 16)
                for i in range(RAW_RING):
                    wait_alone(pool, raw_in[i], (h + 1) * (GROUPS // RAW_RING) * 2 * RB * 16)

        def wait_raw(eng, h, k):
            eng.wait_ge(raw_in[k % RAW_RING],
                        h * (GROUPS // RAW_RING) * 2 * RB * 16 + (k // RAW_RING + 1) * 2 * RB * 16)

        @block.scalar
        def _(act):
            act.sem_inc(mlp_out, MO0)
            act.sem_inc(evacuated, EV0)

            def k_high(n, i, m):
                act.wait_ge(k_in[i], n)
                nc.scalar.activation(ksplit[:, i, 0, :, :].bitcast(F32R), ksplit[:, i, 1, :, :],
                                     ACT.Copy).then_inc(khi_done, 1)

            def evacuate(h, k, first=False):
                act.wait_ge(transposed, h * GROUPS + TR0 + k + 1)
                nc.scalar.activation(pair[:, k, :], tr_ps[:, :], ACT.Copy)
                if not first:
                    act.wait_ge(own_in[k % SPLIT_RING],
                                (h * (GROUPS // SPLIT_RING) + k // SPLIT_RING) * 64)
                nc.scalar.activation(split[:, k % SPLIT_RING, 0, :].bitcast(F32R), tr_ps[:, :],
                                     ACT.Copy).then_inc(evacuated, 1)

            def mlp_step(h, u):
                act.wait_ge(mlp_done, h * MLP_UNITS + u + 1)
                src = kp[(SLOTS + u) % KP_RING]
                if u < N1:
                    nc.scalar.activation(h1_sb[:, u, :], src[:, 0, :], ACT.Relu,
                                         bias=b1_sb[:, u:u + 1]).then_inc(mlp_out, 1)
                elif u < N1 + N2:
                    nc.scalar.activation(h2_sb[:, u - N1, :], src[:, 0, :], ACT.Relu,
                                         bias=b2_sb[:, u - N1:u - N1 + 1]).then_inc(mlp_out, 1)
                else:
                    nc.scalar.activation(y_sb[0:1, bass.ds(h * ROWS, ROWS)], src[0:1, 0, :],
                                         ACT.Copy).then_inc(mlp_out, 1)

            for c in range(K_RING):
                k_high(16, c, c)
            for k in range(EARLY):
                evacuate(0, k, first=True)
            with act.Fori(0, HALVES) as h:
                for j in range(BATCHES):
                    for k in at_batch[j]:
                        evacuate(h, k)
                    if j % CB == 1:
                        dh, c = divmod(j // CB + K_RING, CHUNKS)
                        n = ((h + dh) * (CHUNKS // K_RING) + c // K_RING + 1) * 16
                        in_next_half(act, h, dh, lambda: k_high(n, c % K_RING, c))
                act.wait_ge(weights_in, 5 * 16)
                for u in range(MLP_UNITS):
                    if u < EARLY:
                        with act.If(h < HALVES - 1):
                            evacuate(h + 1, u)
                    mlp_step(h, u)
            act.wait_ge(mlp_out, HALVES * MLP_UNITS + MO0)
            act.dma_start(out, y_sb[0:1, :]).then_inc(y_stored, 16)
            act.wait_ge(y_stored, 16)

        @block.vector
        def _(dve):
            def k_low(n, i):
                dve.wait_ge(khi_done, n)
                nc.vector.tensor_tensor(ksplit[:, i, 1, :, :].bitcast(F32R), ksplit[:, i, 1, :, :],
                                        ksplit[:, i, 0, :, :], ALU.subtract).then_inc(klo_done, 1)

            def g_low(h, k):
                dve.wait_ge(evacuated, h * GROUPS + EV0 + k + 1)
                nc.vector.tensor_tensor(split[:, k % SPLIT_RING, 1, :].bitcast(F32R), pair[:, k, :],
                                        split[:, k % SPLIT_RING, 0, :], ALU.subtract).then_inc(glo_done, 1)

            def add_features(h, c):
                dve.wait_ge(reduced, h * BATCHES + RED0 + (c + 1) * BATCHES_PER_FC)
                nc.vector.tensor_tensor(z_sb[:, c, :], z_ps[:, :], z_sb[:, c, :], ALU.add).then_inc(z_out, 1)

            dve.sem_inc(z_out, Z0)
            k_low(1, 0)
            k_low(2, 1)
            for k in range(EARLY):
                g_low(0, k)
            with dve.Fori(0, HALVES) as h:
                for j in range(BATCHES):
                    for k in at_batch[j]:
                        g_low(h, k)
                    for s in range(BATCH_SLOTS * j, BATCH_SLOTS * (j + 1)):
                        k0, k1 = TILE[SLOT * s][1], TILE[SLOT * s + 1][1]
                        if k0 == k1:
                            factor = pair[:, k0:k0 + 1, :].broadcast_to([P, SLOT, ROWS])
                        else:
                            factor = pair[:, k0:k0 + SLOT, :]
                        dve.wait_ge(kp_done, h * SLOTS + KP0 + s + 1)
                        if s % BATCH_SLOTS == 0:
                            dve.wait_ge(reduced, h * BATCHES + RED0 + j + 1 - P_RING // BATCH_SLOTS)
                        nc.vector.tensor_tensor(prod[:, s % P_RING, :, :], kp[s % KP_RING][:, :, :],
                                                factor, ALU.mult).then_inc(prod_done, 1)
                    if j == BATCHES_PER_FC:
                        dve.wait_ge(dense_in, (h + 1) * 16)
                    if j and j % BATCHES_PER_FC == 0:
                        add_features(h, j // BATCHES_PER_FC - 1)
                    if j % CB == 1:
                        dh, c = divmod(j // CB + K_RING, CHUNKS)
                        in_next_half(dve, h, dh, lambda: k_low((h + dh) * CHUNKS + c + 1, c % K_RING))
                for k in range(EARLY):
                    with dve.If(h < HALVES - 1):
                        g_low(h + 1, k)
                    if k == 0:
                        add_features(h, FC - 1)

        @block.tensor
        def _(pe):
            pe.sem_inc(transposed, TR0)
            pe.sem_inc(kp_done, KP0)
            pe.sem_inc(reduced, RED0)
            pe.wait_ge(consts_ready, 5)

            def transpose_group(h, k):
                wait_raw(pe, h, k)
                pe.wait_ge(evacuated, h * GROUPS + EV0 + k)
                for b in range(RB):
                    last = nc.tensor.transpose(tr_ps[:, b * P:(b + 1) * P],
                                               raw[:, k % RAW_RING, b, :, :].rearrange("p a n -> p (a n)"),
                                               ident[:, :])
                last.then_inc(transposed, 1)

            def kp_free(h, s):
                if s < KP_RING:
                    pe.wait_ge(mlp_out, h * MLP_UNITS + MO0 + s - KP_RING + 1)
                elif s - KP_RING < SLOTS:
                    pe.wait_ge(prod_done, h * SLOTS + s - KP_RING + 1)
                else:
                    pe.wait_ge(mlp_out, h * MLP_UNITS + MO0 + s - KP_RING - SLOTS + 1)

            def products(h, s):
                kp_free(h, s)
                for q in range(SLOT):
                    t = SLOT * s + q
                    o, k = TILE[t]
                    c = t // CHUNK
                    if t % CHUNK == 0:
                        pe.wait_ge(kst_in[c % K_RING], (h * (CHUNKS // K_RING) + c // K_RING + 1) * 64)
                    if o == 0:
                        pe.wait_ge(own_in[k % SPLIT_RING],
                                   (h * (GROUPS // SPLIT_RING) + k // SPLIT_RING + 1) * 64)
                    for part in range(2):
                        last = nc.tensor.matmul(kp[s % KP_RING][:, q, :],
                                                kst[:, c % K_RING, part, t % 2, (t % CHUNK) // 2, :],
                                                own[:, o, :], start=(part == 0), stop=(part == 1))
                last.then_inc(kp_done, 1)

            def reductions(h, j):
                if j % BATCHES_PER_FC == 0:
                    c = j // BATCHES_PER_FC
                    pe.wait_ge(z_out, h * FC + Z0 + c)
                pe.wait_ge(prod_done, h * SLOTS + BATCH_SLOTS * (j + 1))
                for t in range(TILES_PER_BATCH * j, TILES_PER_BATCH * (j + 1)):
                    g = t % 4
                    col = 2 * ((t % (TILES // FC)) // 4)
                    s = t // SLOT
                    last = nc.tensor.matmul(z_ps[32 * g:32 * g + 32, :], ones_sel[:, 30 - col:62 - col],
                                            prod[:, s % P_RING, t % SLOT, :],
                                            start=(j % BATCHES_PER_FC == 0),
                                            stop=(j % BATCHES_PER_FC == BATCHES_PER_FC - 1),
                                            skip_group_check=True)
                last.then_inc(reduced, 1)

            for k in range(EARLY):
                transpose_group(0, k)
            with pe.Fori(0, HALVES) as h:
                for j in range(BATCHES):
                    for k in at_batch[j]:
                        transpose_group(h, k)
                    for s in range(BATCH_SLOTS * j, BATCH_SLOTS * (j + 1)):
                        products(h, s)
                    if j:
                        reductions(h, j - 1)
                with pe.If(h < HALVES - 1):
                    transpose_group(h + 1, 0)
                reductions(h, BATCHES - 1)
                pe.wait_ge(z_out, (h + 1) * FC + Z0)
                pe.wait_ge(weights_in, 5 * 16)
                for u in range(MLP_UNITS):
                    s = SLOTS + u
                    kp_free(h, s)
                    dst = kp[s % KP_RING]
                    if u < N1:
                        for c in range(FC):
                            last = nc.tensor.matmul(dst[:, 0, :], w1_sb[:, c, u * P:(u + 1) * P], z_sb[:, c, :],
                                                    start=(c == 0), stop=(c == FC - 1))
                    elif u < N1 + N2:
                        pe.wait_ge(mlp_out, h * MLP_UNITS + MO0 + N1)
                        n = u - N1
                        for c in range(N1):
                            last = nc.tensor.matmul(dst[:, 0, :], w2_sb[:, c, n * P:(n + 1) * P], h1_sb[:, c, :],
                                                    start=(c == 0), stop=(c == N1 - 1))
                    else:
                        pe.wait_ge(mlp_out, h * MLP_UNITS + MO0 + N1 + N2)
                        for c in range(N2):
                            last = nc.tensor.matmul(dst[0:1, 0, :], w3_sb[:, c:c + 1], h2_sb[:, c, :],
                                                    start=(c == 0), stop=(c == N2 - 1))
                    last.then_inc(mlp_done, 1)
                    if u + 1 < EARLY:
                        with pe.If(h < HALVES - 1):
                            transpose_group(h + 1, u + 1)


def kernel(**inputs):
    import numpy as _np
    import concourse.bacc as _bacc
    from concourse import mybir as _mybir
    from concourse.bass_utils import run_bass_kernel_spmd as _run

    pair_no = {}
    for r in range(FIELDS):
        for c in range(r + 1, FIELDS):
            pair_no[(r, c)] = len(pair_no)
    pairs = len(pair_no)
    k_order = _np.zeros((TILES, 2), _np.int64)
    w1_rows = _np.zeros((FC, P), _np.int64)
    dense = _np.asarray(inputs["dense_ctx"])
    dense_rows = _np.zeros((HALVES, P, FC, ROWS), dense.dtype)
    for t, (o, k) in enumerate(TILE):
        for h in range(2):
            c, row = feature_place(t, h)
            if (o, 2 * k + h) in pair_no:
                k_order[t, h] = pair_no[(o, 2 * k + h)]
                w1_rows[c, row] = pair_no[(o, 2 * k + h)]
            else:
                k_order[t, h] = pairs
                w1_rows[c, row] = pairs + k
                dense_rows[:, row, c, :] = dense[:, k].reshape(HALVES, ROWS)
    kt = _np.asarray(inputs["L0_rec_kernel"]).transpose(2, 1, 0)
    kt = _np.concatenate([kt, _np.zeros((EMBED, 1, EMBED), kt.dtype)], axis=1)
    kt = kt[:, k_order.reshape(-1), :].reshape(EMBED, CHUNKS, CHUNK // 2, 2, 2, EMBED)
    kd = kt.transpose(1, 3, 0, 2, 4, 5).reshape(CHUNKS, P, CHUNK // 2 * P)
    w1 = _np.asarray(inputs["W_top1"])[w1_rows.reshape(-1)].reshape(FC, P, HID1).transpose(1, 0, 2)
    w2 = _np.asarray(inputs["W_top2"]).reshape(N1, P, HID2).transpose(1, 0, 2)
    w3 = _np.asarray(inputs["W_top3"]).reshape(N2, P).transpose(1, 0)
    b1 = _np.asarray(inputs["b_top1"]).reshape(N1, P).transpose(1, 0)
    b2 = _np.asarray(inputs["b_top2"]).reshape(N2, P).transpose(1, 0)
    ids = _np.asarray(inputs["ids"]).reshape(HALVES, RB, P, FIELDS).transpose(0, 2, 1, 3)
    arrays = {
        "dense": dense_rows,
        "ids": ids.reshape(HALVES, P, RB * FIELDS),
    }
    for f in range(FIELDS):
        arrays[f"tbl_{f}"] = _np.asarray(inputs[f"tbl_{f}"])
    arrays.update(kd=kd, w1=w1, b1=b1, w2=w2, b2=b2, w3=w3)

    nc = _bacc.Bacc("TRN2", target_bir_lowering=False, num_devices=1)
    feed, ap = {}, {}
    for name, a in arrays.items():
        a = _np.ascontiguousarray(a)
        feed[f"in_{name}"] = a
        ap[name] = nc.dram_tensor(f"in_{name}", a.shape, _mybir.dt.from_np(a.dtype), kind="ExternalInput").ap()
    out = nc.dram_tensor("out_y", (1, BATCH), _mybir.dt.float32, kind="ExternalOutput").ap()
    pairwise_tower(nc, ap["dense"], ap["ids"], [ap[f"tbl_{f}"] for f in range(FIELDS)], ap["kd"], ap["w1"],
                   ap["b1"], ap["w2"], ap["b2"], ap["w3"], out)
    r = _run(nc, [feed], core_ids=[0])
    return r.results[0]["out_y"].reshape(BATCH, 1)
```

```python
import numpy as np
import concourse.bass as bass
import concourse.mybir as mybir

F32 = mybir.dt.float32
F32R = mybir.dt.float32r
I32 = mybir.dt.int32
ALU = mybir.AluOpType
ACT = mybir.ActivationFunctionType

BATCH, FIELDS, EMBED, DENSE = 1024, 32, 64, 16
HID1, HID2 = 512, 256
P = 128
HALVES = 2
ROWS = BATCH // HALVES
RB = ROWS // P
GROUPS = FIELDS // 2
FOURS = FIELDS // 4
TILES = FIELDS * (FIELDS - 1) // 4
CHUNK = 16
CHUNKS = -(-TILES // CHUNK)
SLOT = 2
SLOTS = TILES // SLOT
BATCH_SLOTS = 2
BATCHES = SLOTS // BATCH_SLOTS
TILES_PER_BATCH = SLOT * BATCH_SLOTS
FC = (2 * TILES + DENSE) // P
BATCHES_PER_FC = P // (2 * TILES_PER_BATCH)
N1, N2 = HID1 // P, HID2 // P
MLP_UNITS = N1 + N2 + 1
KP_RING = 3
PAD = 1
assert (SLOTS + PAD + MLP_UNITS) % KP_RING == 0
P_RING = 4
RAW_RING = 4
SPLIT_RING = 2
LOOKUP = 3
SMALL = 1000
SMALL_P = 125
SMALL_C = SMALL // SMALL_P
ACT_HOTS = 1
HOT_RING = 2
PARTS_RING = 4
AHEAD = 4
K_RING = 2
DENSE_AT, WEIGHTS_AT = 12, 40
LEAD = {k: 2 if k < 6 else 3 if k < 12 else 4 for k in range(GROUPS)}

def tile_order():
    order = []
    for k in range(GROUPS):
        m = k // 2
        if k % 2 == 0:
            order += [(o, k, None) for o in range(4 * m)]
            if m:
                order.append((4 * (m - 1) + 1, GROUPS, m - 1))
                late = (4 * (m - 1) + 2, GROUPS + 1, m - 1)
        else:
            owners = list(range(4 * m + 1))
            if m and len(order) % 2 == 0:
                order.append((owners.pop(0), k, None))
            if m:
                order.append(late)
            order += [(o, k, None) for o in owners]
    m = FOURS - 1
    return order + [(4 * m + 1, GROUPS, m), (4 * m + 2, GROUPS + 1, m)]


TILE = tile_order()
assert len(TILE) == TILES


def partners(t):
    o, k, m = TILE[t]
    return (2 * k, 2 * k + 1) if m is None else (4 * m + k - GROUPS, 4 * m + 3)


assert len({frozenset((TILE[t][0], f)) for t in range(TILES) for f in partners(t)}) == 2 * TILES


def first_batch(k):
    return min(t for t, (o, f, m) in enumerate(TILE) if f == k) // TILES_PER_BATCH


def mixed_tiles(m):
    return [t for t in range(TILES) if TILE[t][2] == m]


def groups_at():
    at = [[] for _ in range(BATCHES)]
    for k in range(AHEAD, GROUPS):
        at[max(0, first_batch(k) - LEAD[k])].append(k)
    assert [k for now in at for k in now] == list(range(AHEAD, GROUPS))
    return at


def feature_place(t, h):
    c, i = divmod(t, P // 2)
    return c, 32 * (i % 4) + 2 * (i // 4) + h


def dense_row(n):
    left = 32 - 2 * BATCHES + 2 * BATCHES_PER_FC * (FC - 1)
    return 32 * (n // left) + 32 - left + n % left


def pairwise_tower(nc, dense, ids, first_ids, row_no, tables, kd, w1, b1, w2, b2, w3, out):
    from contextlib import ExitStack
    ctx = ExitStack()
    with ctx:
        def sb(name, shape, dt=F32):
            return ctx.enter_context(nc.sbuf_tensor(name, shape, dt))

        def sem(name):
            return ctx.enter_context(nc.semaphore(name))

        ids_sb = sb("ids_sb", [P, RB * FIELDS], I32)
        raw = sb("raw", [P, RAW_RING, RB, 2, EMBED])
        split = sb("split", [P, SPLIT_RING, 2, ROWS])
        own = sb("own", [P, FIELDS, ROWS], F32R)
        pair = sb("pair", [P, GROUPS + 2, ROWS])
        ksplit = sb("ksplit", [P, K_RING, 2, CHUNK // 2, P])
        kst = sb("kst", [P, K_RING, 2, 2, CHUNK // 2, P], F32R)
        prod = sb("prod", [P, P_RING, SLOT, ROWS])
        z_sb = sb("z_sb", [P, FC, ROWS])
        w1_sb = sb("w1_sb", [P, FC, HID1])
        w2_sb = sb("w2_sb", [P, N1, HID2])
        w3_sb = sb("w3_sb", [P, N2])
        b1_sb = sb("b1_sb", [P, N1])
        b2_sb = sb("b2_sb", [P, N2])
        ident = sb("ident", [P, P])
        ones_sel = sb("ones_sel", [P, 64])
        y_sb = sb("y_sb", [1, BATCH])
        row_sb = sb("row_sb", [P, SMALL_C])
        fold = sb("fold", [P, 3 * EMBED], F32R)
        h1_sb = prod[:, 0:2, :, :].rearrange("p a b n -> p (a b) n")
        h2_sb = prod[:, 2, :, :]
        LF = 2 * LOOKUP
        onehot = [own[:, at:at + SMALL_C, :] for at in (2 * AHEAD, 2 * AHEAD + SMALL_C)]
        table_parts = own[:, FIELDS - 2 * PARTS_RING:, :].rearrange("p (f a) n -> p f (a n)", a=2).rearrange(
            "p f (c n) -> p f c n", n=P)
        table_raw = pair[:, 4:4 + LF, :].rearrange("p f (c n) -> p f c n", n=EMBED)
        ids_all = pair[:, GROUPS - LF:GROUPS, :].bitcast(I32)

        kp = [ctx.enter_context(nc.psum_tensor(f"kp{i}", [P, SLOT, ROWS], F32)) for i in range(KP_RING)]
        z_ps = ctx.enter_context(nc.psum_tensor("z_ps", [P, ROWS], F32))
        tr_ps = ctx.enter_context(nc.psum_tensor("tr_ps", [P, ROWS], F32))

        weights_in = sem("weights_in")
        dense_in = sem("dense_in")
        mixed_in = sem("mixed_in")
        mixed_copied = sem("mixed_copied")
        ids_in = sem("ids_in")
        raw_in = [sem(f"raw_in{i}") for i in range(RAW_RING)]
        k_in = [sem(f"k_in{i}") for i in range(K_RING)]
        kst_in = [sem(f"kst_in{i}") for i in range(K_RING)]
        consts_ready = sem("consts_ready")
        khi_done = sem("khi_done")
        klo_done = sem("klo_done")
        row_no_in = sem("row_no_in")
        lookup_ids_in = [sem(f"lookup_ids_in{f}") for f in range(LF)]
        table_in = [sem(f"table_in{f}") for f in range(LF)]
        table_hi = sem("table_hi")
        table_lo = sem("table_lo")
        onehot_ready = sem("onehot_ready")
        distance_ready = sem("distance_ready")
        act_onehots = sem("act_onehots")
        onehot_used = sem("onehot_used")
        looked_up = sem("looked_up")
        lookup_out = sem("lookup_out")
        fold_ready = sem("fold_ready")
        own_in = [sem(f"own_in{i}") for i in range(SPLIT_RING)]
        glo_done = sem("glo_done")
        transposed = sem("transposed")
        evacuated = sem("evacuated")
        kp_done = sem("kp_done")
        prod_done = sem("prod_done")
        reduced = sem("reduced")
        z_out = sem("z_out")
        mlp_done = sem("mlp_done")
        mlp_out = sem("mlp_out")
        y_stored = sem("y_stored")
        passed = sem("passed")

        TR0 = RAW_RING
        KP0 = CHUNK // SLOT
        RED0 = P_RING // BATCH_SLOTS
        MO0 = MLP_UNITS
        EV0 = Z0 = 1
        OWN0 = [64 * len(range(i, LOOKUP, SPLIT_RING)) for i in range(SPLIT_RING)]
        RAW_SKIPPED = [len(range(i, LOOKUP, RAW_RING)) for i in range(RAW_RING)]
        CB = CHUNK // TILES_PER_BATCH

        def wait_alone(eng, signal, n):
            eng.wait_ge(signal, n)
            eng.sem_inc(passed, 1)

        PAIR_OUT = [3 * k + 4 for k in range(LOOKUP - 1)] + [3 * LOOKUP]
        assert LOOKUP == 3 <= AHEAD
        at_batch = groups_at()
        mixed_at = {mixed_tiles(m - 1)[-1] // TILES_PER_BATCH + 2: m for m in range(1, FOURS)}
        KD2 = kd.rearrange("c p (m n) -> c p m n", n=P)

        def in_next_half(eng, h, other_half, step):
            if other_half:
                with eng.If(h < HALVES - 1):
                    step()
            else:
                step()

        def groups_now(h, j, step):
            for k in at_batch[j]:
                step(h, k)

        def load_table(eng, f):
            eng.dma_start(table_raw[0:SMALL_P, f, :, :],
                          tables[f].rearrange("(p c) n -> p c n", c=SMALL_C)).then_inc(table_in[f], 16)

        block = ctx.enter_context(nc.Block())

        @block.sync
        def _(sp):
            def load_k(c):
                sp.dma_start(ksplit[:, c % K_RING, 1, :, :], KD2[c]).then_inc(k_in[c % K_RING], 16)

            def load_dense(h):
                sp.dma_start(z_sb[:, FC - 1, :], dense[h]).then_inc(dense_in, 16)

            def mix_b(m):
                sp.dma_start(pair[0:64, GROUPS + 1, :], pair[64:128, 2 * m, :]).then_inc(mixed_in, 16)

            def spread_k(h, c):
                i = c % K_RING
                wait_alone(sp, klo_done, h * CHUNKS + c + 1)
                for q in range(2):
                    for half in range(2):
                        sp.dma_start(kst[64 * half:64 * half + 64, i, :, q, :, :].bitcast(F32),
                                     ksplit[64 * q:64 * q + 64, i, :, :, :]).then_inc(kst_in[i], 16)

            def spread_own(h, k):
                wait_alone(sp, glo_done, h * GROUPS + k + 1)
                for n in range(2):
                    for part in range(2):
                        sp.dma_start(own[64 * part:64 * part + 64, 2 * k + n, :].bitcast(F32),
                                     split[64 * n:64 * n + 64, k % SPLIT_RING, part, :],
                                     ).then_inc(own_in[k % SPLIT_RING], 16)

            def load_weights():
                sp.dma_start(w1_sb[:, :, :], w1).then_inc(weights_in, 16)
                sp.dma_start(w2_sb[:, :, :], w2).then_inc(weights_in, 16)
                sp.dma_start(w3_sb[:, :], w3).then_inc(weights_in, 16)
                sp.dma_start(b1_sb[:, :], b1).then_inc(weights_in, 16)
                sp.dma_start(b2_sb[:, :], b2).then_inc(weights_in, 16)

            def spread_read(h, c):
                wait_alone(sp, kst_in[c % K_RING], (h * (CHUNKS // K_RING) + c // K_RING + 1) * 64)

            for i in range(SPLIT_RING):
                sp.sem_inc(own_in[i], OWN0[i])
            for f in range(LF):
                sp.dma_start(ids_all[:, f, :], first_ids[f:f + 1, :].broadcast_to([P, ROWS]))\
                  .then_inc(lookup_ids_in[f], 16)
                if f == 0:
                    sp.dma_start(row_sb[:, :], row_no).then_inc(row_no_in, 16)
                if f >= 2:
                    load_table(sp, f)
                if f == 2:
                    load_k(0)
            load_k(1)
            spread_k(0, 0)
            spread_read(0, 0)
            load_k(K_RING)
            sp.wait_ge(lookup_out, PAIR_OUT[1])
            mix_b(0)
            for k in range(LOOKUP, AHEAD):
                spread_own(0, k)
            spread_k(0, 1)
            sp.wait_ge(onehot_used, LF * SMALL_C)
            with sp.Fori(0, HALVES) as h:
                for j in range(BATCHES):
                    if j % CB == 0:
                        dh, c = divmod(j // CB + 1, CHUNKS)

                        def next_spread():
                            wait_alone(sp, kp_done, h * SLOTS + KP0 + j // CB * CHUNK // SLOT)
                            spread_k(h + dh, c)
                        if j == 0:
                            with sp.If(h > 0):
                                next_spread()
                        else:
                            in_next_half(sp, h, dh, next_spread)
                    groups_now(h, j, spread_own)
                    if j in mixed_at:
                        m = mixed_at[j]
                        wait_alone(sp, glo_done, h * GROUPS + 2 * m + 2)
                        wait_alone(sp, prod_done, h * SLOTS + mixed_tiles(m - 1)[-1] // SLOT + 1)
                        mix_b(m)
                    if j == DENSE_AT:
                        with sp.If(h < 1):
                            load_dense(0)
                    if j == WEIGHTS_AT:
                        with sp.If(h < 1):
                            load_weights()
                    if j % CB == 2:
                        dh, c = divmod(j // CB + 1, CHUNKS)
                        dn, n = divmod(j // CB + 1 + K_RING, CHUNKS)

                        def next_load():
                            spread_read(h + dh, c)
                            load_k(n)
                        in_next_half(sp, h, dn, next_load)
                with sp.If(h < HALVES - 1):
                    spread_read(h + 1, 0)
                    load_k(K_RING)
                    for k in range(AHEAD):
                        spread_own(h + 1, k)
                        if k == 1:
                            wait_alone(sp, prod_done, (h + 1) * SLOTS)
                            mix_b(0)
                    wait_alone(sp, mlp_done, h * MLP_UNITS + N1)
                    load_dense(HALVES - 1)

        @block.gpsimd
        def _(pool):
            def gather(h, k):
                wait_alone(pool, transposed, h * GROUPS + TR0 + k - RAW_RING + 1)
                for n in range(2):
                    f = 2 * k + n
                    for b in range(RB):
                        col = b * FIELDS + f
                        nc.gpsimd.indirect_dma_start(
                            raw[:, k % RAW_RING, b, n, :], None, tables[f],
                            bass.IndirectOffsetOnAxis(ap=ids_sb[:, col:col + 1], axis=0),
                        ).then_inc(raw_in[k % RAW_RING], 16)

            pool.dma_start(ids_sb[:, :], ids[0]).then_inc(ids_in, 16)
            nc.gpsimd.memset(ident[:, :], 0.0).then_inc(consts_ready, 1)
            nc.gpsimd.memset(ones_sel[:, :], 0.0).then_inc(consts_ready, 1)
            pool.wait_ge(consts_ready, 2)
            nc.gpsimd.affine_select(out=ident[:, :], in_=ident[:, :], compare_op=ALU.not_equal, fill=1.0,
                                    base=0, pattern=[[-1, P]], channel_multiplier=1).then_inc(consts_ready, 1)
            pool.wait_ge(consts_ready, 3)
            nc.gpsimd.memset(ones_sel[0:64, 30:31], 1.0).then_inc(consts_ready, 1)
            pool.wait_ge(consts_ready, 4)
            nc.gpsimd.memset(ones_sel[64:128, 31:32], 1.0).then_inc(consts_ready, 1)
            pool.wait_ge(consts_ready, 5)
            with pool.Fori(0, HALVES) as h:
                wait_alone(pool, ids_in, h * 16 + 16)
                with pool.If(h > 0):
                    for k in range(LOOKUP):
                        gather(h, k)
                for k in range(LOOKUP, GROUPS):
                    gather(h, k)
                with pool.If(h < HALVES - 1):
                    for i in range(RAW_RING):
                        wait_alone(pool, raw_in[i],
                                   ((h + 1) * (GROUPS // RAW_RING) - RAW_SKIPPED[i]) * 2 * RB * 16)
                    pool.dma_start(ids_sb[:, :], ids[HALVES - 1]).then_inc(ids_in, 16)

        def wait_raw(eng, h, k):
            i = k % RAW_RING
            eng.wait_ge(raw_in[i], (h * (GROUPS // RAW_RING) + k // RAW_RING + 1 - RAW_SKIPPED[i]) * 2 * RB * 16)

        @block.scalar
        def _(act):
            act.sem_inc(mlp_out, MO0)
            act.sem_inc(evacuated, EV0 + LOOKUP)

            def k_high(n, i, m):
                act.wait_ge(k_in[i], n)
                nc.scalar.activation(ksplit[:, i, 0, :, :].bitcast(F32R), ksplit[:, i, 1, :, :],
                                     ACT.Copy).then_inc(khi_done, 1)

            def evacuate(h, k):
                act.wait_ge(transposed, h * GROUPS + TR0 + k + 1)
                nc.scalar.activation(pair[:, k, :], tr_ps[:, :], ACT.Copy)
                act.wait_ge(own_in[k % SPLIT_RING],
                            (h * (GROUPS // SPLIT_RING) + k // SPLIT_RING) * 64)
                nc.scalar.activation(split[:, k % SPLIT_RING, 0, :].bitcast(F32R), tr_ps[:, :],
                                     ACT.Copy).then_inc(evacuated, 1)

            def mlp_step(h, u):
                act.wait_ge(mlp_done, h * MLP_UNITS + u + 1)
                src = kp[(SLOTS + PAD + u) % KP_RING]
                if u < N1:
                    nc.scalar.activation(h1_sb[:, u, :], src[:, 0, :], ACT.Relu,
                                         bias=b1_sb[:, u:u + 1]).then_inc(mlp_out, 1)
                elif u < N1 + N2:
                    nc.scalar.activation(h2_sb[:, u - N1, :], src[:, 0, :], ACT.Relu,
                                         bias=b2_sb[:, u - N1:u - N1 + 1]).then_inc(mlp_out, 1)
                else:
                    nc.scalar.activation(y_sb[0:1, bass.ds(h * ROWS, ROWS)], src[0:1, 0, :],
                                         ACT.Copy).then_inc(mlp_out, 1)

            def field_out(f):
                act.wait_ge(looked_up, f + 1 + max(0, f - 1) // 2)
                nc.scalar.activation(own[:, f, :], kp[f // 2][:, f % 2, :], ACT.Copy).then_inc(lookup_out, 1)

            def pair_out(k):
                act.wait_ge(looked_up, min(3 * k + 4, 3 * LOOKUP))
                nc.scalar.activation(pair[:, k, :], z_ps[:, :], ACT.Copy).then_inc(lookup_out, 1)

            def mix_ad(m):
                nc.scalar.activation(pair[0:64, GROUPS, :], pair[0:64, 2 * m, :],
                                     ACT.Copy).then_inc(mixed_copied, 1)
                nc.scalar.activation(pair[64:128, GROUPS:GROUPS + 2, :],
                                     pair[64:128, 2 * m + 1:2 * m + 2, :].broadcast_to([64, 2, ROWS]),
                                     ACT.Copy).then_inc(mixed_copied, 1)

            def features_out(h, c):
                act.wait_ge(reduced, h * BATCHES + RED0 + (c + 1) * BATCHES_PER_FC)
                nc.scalar.activation(z_sb[:, c, :], z_ps[:, :], ACT.Copy).then_inc(z_out, 1)

            load_table(act, 0)
            load_table(act, 1)
            act.wait_ge(row_no_in, 16)
            for f in range(LF):
                hot = onehot[f % HOT_RING]
                act.wait_ge(lookup_ids_in[f], 16)
                for c in range(SMALL_C - ACT_HOTS, SMALL_C):
                    if f >= HOT_RING:
                        act.wait_ge(onehot_used, (f - HOT_RING) * SMALL_C + c + 1)
                    nc.scalar.activation(hot[0:SMALL_P, c, :], ids_all[0:SMALL_P, f, :], ACT.Abs, scale=-1.0,
                                         bias=row_sb[0:SMALL_P, c:c + 1]).then_inc(distance_ready, 1)
                act.wait_ge(distance_ready, (f + 1) * ACT_HOTS)
                nc.scalar.activation(hot[0:SMALL_P, SMALL_C - ACT_HOTS:SMALL_C, :],
                                     hot[0:SMALL_P, SMALL_C - ACT_HOTS:SMALL_C, :].bitcast(F32), ACT.Relu,
                                     scale=-1.0, bias=1.0).then_inc(act_onehots, 1)
                act.wait_ge(table_in[f], 16)
                if f >= PARTS_RING:
                    act.wait_ge(onehot_used, (f - PARTS_RING + 1) * SMALL_C)
                nc.scalar.activation(table_parts[0:SMALL_P, f % PARTS_RING, :, 0:EMBED],
                                     table_raw[0:SMALL_P, f, :, :], ACT.Copy).then_inc(table_hi, 1)
                if 1 <= f <= K_RING:
                    k_high(16, f - 1, f - 1)
                if f == LF - 1:
                    for k in range(LOOKUP, AHEAD):
                        evacuate(0, k)
                if f:
                    field_out(f - 1)
                if f >= 3 and f % 2:
                    pair_out((f - 3) // 2)
                if f == LF - 1:
                    act.wait_ge(lookup_out, PAIR_OUT[1])
                    mix_ad(0)
            field_out(LF - 1)
            pair_out(LOOKUP - 1)
            with act.Fori(0, HALVES) as h:
                for j in range(BATCHES):
                    groups_now(h, j, evacuate)
                    if j in mixed_at:
                        m = mixed_at[j]
                        act.wait_ge(evacuated, h * GROUPS + EV0 + 2 * m + 2)
                        act.wait_ge(prod_done, h * SLOTS + mixed_tiles(m - 1)[-1] // SLOT + 1)
                        mix_ad(m)
                    if j and j % BATCHES_PER_FC == 0:
                        features_out(h, j // BATCHES_PER_FC - 1)
                    if j % CB == 1:
                        dh, c = divmod(j // CB + K_RING, CHUNKS)
                        n = ((h + dh) * (CHUNKS // K_RING) + c // K_RING + 1) * 16
                        in_next_half(act, h, dh, lambda: k_high(n, c % K_RING, c))
                act.wait_ge(weights_in, 5 * 16)
                for u in range(MLP_UNITS):
                    if u < AHEAD:
                        with act.If(h < HALVES - 1):
                            evacuate(h + 1, u)
                            if u == 1:
                                act.wait_ge(evacuated, (h + 1) * GROUPS + EV0 + 2)
                                act.wait_ge(prod_done, (h + 1) * SLOTS)
                                mix_ad(0)
                    mlp_step(h, u)
            act.wait_ge(mlp_out, HALVES * MLP_UNITS + MO0)
            act.dma_start(out, y_sb[0:1, :]).then_inc(y_stored, 16)
            act.wait_ge(y_stored, 16)

        @block.vector
        def _(dve):
            def k_low(n, i):
                dve.wait_ge(khi_done, n)
                nc.vector.tensor_tensor(ksplit[:, i, 1, :, :].bitcast(F32R), ksplit[:, i, 1, :, :],
                                        ksplit[:, i, 0, :, :], ALU.subtract).then_inc(klo_done, 1)

            def g_low(h, k):
                dve.wait_ge(evacuated, h * GROUPS + EV0 + k + 1)
                nc.vector.tensor_tensor(split[:, k % SPLIT_RING, 1, :].bitcast(F32R), pair[:, k, :],
                                        split[:, k % SPLIT_RING, 0, :], ALU.subtract).then_inc(glo_done, 1)

            def add_last_features(h):
                dve.wait_ge(reduced, (h + 1) * BATCHES + RED0)
                dve.wait_ge(dense_in, (h + 1) * 16)
                nc.vector.tensor_tensor(z_sb[:, FC - 1, :], z_ps[:, :], z_sb[:, FC - 1, :],
                                        ALU.add).then_inc(z_out, 1)

            dve.sem_inc(z_out, Z0)
            dve.sem_inc(glo_done, LOOKUP)
            dve.wait_ge(consts_ready, 5)
            nc.vector.memset(fold[:, :].bitcast(F32), 0.0).then_inc(fold_ready, 1)
            dve.wait_ge(fold_ready, 1)
            nc.vector.tensor_tensor(fold[:, EMBED:2 * EMBED], ident[:, 0:EMBED], ident[:, EMBED:P],
                                    ALU.add).then_inc(fold_ready, 1)
            dve.wait_ge(row_no_in, 16)
            for f in range(LF):
                dve.wait_ge(lookup_ids_in[f], 16)
                for c in range(SMALL_C - ACT_HOTS):
                    if f >= HOT_RING:
                        dve.wait_ge(onehot_used, (f - HOT_RING) * SMALL_C + c + 1)
                    nc.vector.tensor_scalar(onehot[f % HOT_RING][0:SMALL_P, c, :], ids_all[0:SMALL_P, f, :],
                                            row_sb[0:SMALL_P, c:c + 1], None,
                                            ALU.is_equal).then_inc(onehot_ready, 1)
                dve.wait_ge(table_hi, f + 1)
                nc.vector.tensor_tensor(table_parts[0:SMALL_P, f % PARTS_RING, :, EMBED:P],
                                        table_raw[0:SMALL_P, f, :, :],
                                        table_parts[0:SMALL_P, f % PARTS_RING, :, 0:EMBED].bitcast(F32),
                                        ALU.subtract).then_inc(table_lo, 1)
                if f == 2:
                    k_low(1, 0)
            for k in range(LOOKUP, AHEAD):
                g_low(0, k)
            k_low(2, 1)
            dve.wait_ge(lookup_out, 3 * LOOKUP)
            with dve.Fori(0, HALVES) as h:
                for j in range(BATCHES):
                    groups_now(h, j, g_low)
                    for s in range(BATCH_SLOTS * j, BATCH_SLOTS * (j + 1)):
                        (o0, k0, m0), (o1, k1, m1) = TILE[SLOT * s:SLOT * (s + 1)]
                        if k0 == k1:
                            factor = pair[:, k0:k0 + 1, :].broadcast_to([P, SLOT, ROWS])
                        else:
                            factor = pair[:, k0:k1 + 1:k1 - k0, :]
                        if k0 == GROUPS or k1 == GROUPS:
                            m = m1 if m0 is None else m0
                            dve.wait_ge(mixed_in, (h * FOURS + m + 1) * 16)
                            dve.wait_ge(mixed_copied, (h * FOURS + m + 1) * 2)
                        dve.wait_ge(kp_done, h * SLOTS + KP0 + s + 1)
                        if s % BATCH_SLOTS == 0:
                            dve.wait_ge(reduced, h * BATCHES + RED0 + j + 1 - P_RING // BATCH_SLOTS)
                        nc.vector.tensor_tensor(prod[:, s % P_RING, :, :], kp[s % KP_RING][:, :, :],
                                                factor, ALU.mult).then_inc(prod_done, 1)
                    if j % CB == 1:
                        dh, c = divmod(j // CB + K_RING, CHUNKS)
                        in_next_half(dve, h, dh, lambda: k_low((h + dh) * CHUNKS + c + 1, c % K_RING))
                for k in range(AHEAD):
                    with dve.If(h < HALVES - 1):
                        g_low(h + 1, k)
                    if k == 0:
                        add_last_features(h)

        @block.tensor
        def _(pe):
            pe.sem_inc(transposed, TR0 + LOOKUP)
            pe.sem_inc(kp_done, KP0)
            pe.sem_inc(reduced, RED0)
            pe.wait_ge(consts_ready, 5)

            def transpose_group(h, k):
                wait_raw(pe, h, k)
                pe.wait_ge(evacuated, h * GROUPS + EV0 + k)
                for b in range(RB):
                    last = nc.tensor.transpose(tr_ps[:, b * P:(b + 1) * P],
                                               raw[:, k % RAW_RING, b, :, :].rearrange("p a n -> p (a n)"),
                                               ident[:, :])
                last.then_inc(transposed, 1)

            def kp_free(h, s):
                if s < KP_RING:
                    pe.wait_ge(mlp_out, h * MLP_UNITS + MO0 + s - KP_RING + 1)
                elif s - KP_RING < SLOTS:
                    pe.wait_ge(prod_done, h * SLOTS + s - KP_RING + 1)
                elif s - KP_RING >= SLOTS + PAD:
                    pe.wait_ge(mlp_out, h * MLP_UNITS + MO0 + s - KP_RING - SLOTS - PAD + 1)

            def products(h, s):
                kp_free(h, s)
                for q in range(SLOT):
                    t = SLOT * s + q
                    o = TILE[t][0]
                    k = o // 2
                    c = t // CHUNK
                    if t % CHUNK == 0:
                        pe.wait_ge(kst_in[c % K_RING], (h * (CHUNKS // K_RING) + c // K_RING + 1) * 64)
                    if all(tile[0] // 2 != k for tile in TILE[:t]):
                        pe.wait_ge(own_in[k % SPLIT_RING],
                                   (h * (GROUPS // SPLIT_RING) + k // SPLIT_RING + 1) * 64)
                    for part in range(2):
                        last = nc.tensor.matmul(kp[s % KP_RING][:, q, :],
                                                kst[:, c % K_RING, part, t % 2, (t % CHUNK) // 2, :],
                                                own[:, o, :], start=(part == 0), stop=(part == 1))
                last.then_inc(kp_done, 1)

            def reductions(h, j):
                if j % BATCHES_PER_FC == 0:
                    if j == 0:
                        pe.wait_ge(lookup_out, 3 * LOOKUP)
                    c = j // BATCHES_PER_FC
                    pe.wait_ge(z_out, h * FC + Z0 + c)
                pe.wait_ge(prod_done, h * SLOTS + BATCH_SLOTS * (j + 1))
                for t in range(TILES_PER_BATCH * j, TILES_PER_BATCH * (j + 1)):
                    g = t % 4
                    col = 2 * ((t % (P // 2)) // 4)
                    s = t // SLOT
                    last = nc.tensor.matmul(z_ps[32 * g:32 * g + 32, :], ones_sel[:, 30 - col:62 - col],
                                            prod[:, s % P_RING, t % SLOT, :],
                                            start=(j % BATCHES_PER_FC == 0),
                                            stop=(j % BATCHES_PER_FC == BATCHES_PER_FC - 1
                                                  or j == BATCHES - 1),
                                            skip_group_check=True)
                last.then_inc(reduced, 1)

            def fold_pair(k):
                pe.wait_ge(fold_ready, 2)
                pe.wait_ge(lookup_out, 3 * k + 2)
                for n in range(2):
                    last = nc.tensor.matmul(z_ps[:, :], fold[:, EMBED * (1 - n):EMBED * (1 - n) + P],
                                            own[:, 2 * k + n, :], start=(n == 0), stop=(n == 1))
                last.then_inc(looked_up, 1)

            for k in range(LOOKUP):
                for n in range(2):
                    f = 2 * k + n
                    pe.wait_ge(table_lo, f + 1)
                    for c in range(SMALL_C):
                        if c < SMALL_C - ACT_HOTS:
                            pe.wait_ge(onehot_ready, f * (SMALL_C - ACT_HOTS) + c + 1)
                        else:
                            pe.wait_ge(act_onehots, f + 1)
                        nc.tensor.matmul(kp[k][:, n, :], table_parts[0:SMALL_P, f % PARTS_RING, c, :],
                                         onehot[f % HOT_RING][0:SMALL_P, c, :], start=(c == 0),
                                         stop=(c == SMALL_C - 1)).then_inc(onehot_used, 1)
                    pe.wait_ge(onehot_used, (f + 1) * SMALL_C)
                    pe.sem_inc(looked_up, 1)
                    if f and f % 2 == 0:
                        fold_pair(k - 1)
                    if f == LF - 3:
                        for g in range(LOOKUP, AHEAD):
                            transpose_group(0, g)
            fold_pair(LOOKUP - 1)
            with pe.Fori(0, HALVES) as h:
                for j in range(BATCHES):
                    groups_now(h, j, transpose_group)
                    for s in range(BATCH_SLOTS * j, BATCH_SLOTS * (j + 1)):
                        products(h, s)
                    if j:
                        reductions(h, j - 1)
                with pe.If(h < HALVES - 1):
                    transpose_group(h + 1, 0)
                reductions(h, BATCHES - 1)
                pe.wait_ge(weights_in, 5 * 16)
                for u in range(MLP_UNITS):
                    s = SLOTS + PAD + u
                    kp_free(h, s)
                    dst = kp[s % KP_RING]
                    if u < N1:
                        for c in range(FC):
                            if u == 0:
                                pe.wait_ge(z_out, h * FC + Z0 + c + 1)
                            last = nc.tensor.matmul(dst[:, 0, :], w1_sb[:, c, u * P:(u + 1) * P], z_sb[:, c, :],
                                                    start=(c == 0), stop=(c == FC - 1))
                    elif u < N1 + N2:
                        n = u - N1
                        for c in range(N1):
                            if n == 0:
                                pe.wait_ge(mlp_out, h * MLP_UNITS + MO0 + c + 1)
                            last = nc.tensor.matmul(dst[:, 0, :], w2_sb[:, c, n * P:(n + 1) * P], h1_sb[:, c, :],
                                                    start=(c == 0), stop=(c == N1 - 1))
                    else:
                        for c in range(N2):
                            pe.wait_ge(mlp_out, h * MLP_UNITS + MO0 + N1 + c + 1)
                            last = nc.tensor.matmul(dst[0:1, 0, :], w3_sb[:, c:c + 1], h2_sb[:, c, :],
                                                    start=(c == 0), stop=(c == N2 - 1))
                    last.then_inc(mlp_done, 1)
                    if u + 1 < AHEAD:
                        with pe.If(h < HALVES - 1):
                            transpose_group(h + 1, u + 1)


def kernel(**inputs):
    import numpy as _np
    import concourse.bacc as _bacc
    from concourse import mybir as _mybir
    from concourse.bass_utils import run_bass_kernel_spmd as _run

    tables = [_np.asarray(inputs[f"tbl_{f}"]) for f in range(FIELDS)]
    small = [f for f in range(FIELDS) if tables[f].shape[0] == SMALL][:2 * LOOKUP]
    order = small + [f for f in range(FIELDS) if f not in small]
    pair_no = {}
    for r in range(FIELDS):
        for c in range(r + 1, FIELDS):
            pair_no[(r, c)] = len(pair_no)
    pairs = len(pair_no)
    k_order = _np.full((CHUNKS * CHUNK, 2), 2 * pairs, _np.int64)
    w1_rows = _np.zeros((FC, P), _np.int64)
    for t in range(TILES):
        for h in range(2):
            owner, partner = order[TILE[t][0]], order[partners(t)[h]]
            p = pair_no[(min(owner, partner), max(owner, partner))]
            k_order[t, h] = p if owner < partner else pairs + p
            w1_rows[feature_place(t, h)] = p
    dense = _np.asarray(inputs["dense_ctx"])
    dense_rows = _np.zeros((HALVES, P, ROWS), dense.dtype)
    for n in range(DENSE):
        w1_rows[FC - 1, dense_row(n)] = pairs + n
        dense_rows[:, dense_row(n)] = dense[:, n].reshape(HALVES, ROWS)
    kin = _np.asarray(inputs["L0_rec_kernel"])
    kt = _np.concatenate([kin.transpose(2, 1, 0), kin, _np.zeros((EMBED, 1, EMBED), kin.dtype)], axis=1)
    kt = kt[:, k_order.reshape(-1), :].reshape(EMBED, CHUNKS, CHUNK // 2, 2, 2, EMBED)
    kd = kt.transpose(1, 3, 0, 2, 4, 5).reshape(CHUNKS, P, CHUNK // 2 * P)
    w1 = _np.asarray(inputs["W_top1"])[w1_rows.reshape(-1)].reshape(FC, P, HID1).transpose(1, 0, 2)
    w2 = _np.asarray(inputs["W_top2"]).reshape(N1, P, HID2).transpose(1, 0, 2)
    w3 = _np.asarray(inputs["W_top3"]).reshape(N2, P).transpose(1, 0)
    b1 = _np.asarray(inputs["b_top1"]).reshape(N1, P).transpose(1, 0)
    b2 = _np.asarray(inputs["b_top2"]).reshape(N2, P).transpose(1, 0)
    ids = _np.asarray(inputs["ids"])[:, order]
    first_ids = ids[:ROWS, :2 * LOOKUP].transpose(1, 0)
    row_no = _np.arange(P * SMALL_C, dtype=_np.float32).reshape(P, SMALL_C)
    ids = ids.reshape(HALVES, RB, P, FIELDS).transpose(0, 2, 1, 3)
    arrays = {
        "dense": dense_rows,
        "ids": ids.reshape(HALVES, P, RB * FIELDS), "first_ids": first_ids, "row_no": row_no,
    }
    for f in range(FIELDS):
        arrays[f"tbl_{f}"] = tables[f]
    arrays.update(kd=kd, w1=w1, b1=b1, w2=w2, b2=b2, w3=w3)

    nc = _bacc.Bacc("TRN2", target_bir_lowering=False, num_devices=1)
    feed, ap = {}, {}
    for name, a in arrays.items():
        a = _np.ascontiguousarray(a)
        feed[f"in_{name}"] = a
        ap[name] = nc.dram_tensor(f"in_{name}", a.shape, _mybir.dt.from_np(a.dtype), kind="ExternalInput").ap()
    out = nc.dram_tensor("out_y", (1, BATCH), _mybir.dt.float32, kind="ExternalOutput").ap()
    pairwise_tower(nc, ap["dense"], ap["ids"], ap["first_ids"], ap["row_no"],
                   [ap[f"tbl_{f}"] for f in order], ap["kd"], ap["w1"],
                   ap["b1"], ap["w2"], ap["b2"], ap["w3"], out)
    r = _run(nc, [feed], core_ids=[0])
    return r.results[0]["out_y"].reshape(BATCH, 1)
```
